# Optimizing a Trainium2 kernel written in Bass

```python
import numpy as np
import jax
import jax.numpy as jnp

def _softmax(x, axis=-1):
    return jax.nn.softmax(x, axis=axis)

def _gelu(x):
    return jax.nn.gelu(x, approximate=True)

def _silu(x):
    return jax.nn.silu(x)

def _sigmoid(x):
    return jax.nn.sigmoid(x)

def _layernorm(x, axis=-1, eps=1e-05):
    m = jnp.mean(x, axis=axis, keepdims=True)
    v = jnp.var(x, axis=axis, keepdims=True)
    return (x - m) / jnp.sqrt(v + eps)

def _scatter_add(tgt, idx, src, axis=0):
    return tgt.at[idx].add(src)

def _segment_sum(src, seg, n):
    return jax.ops.segment_sum(src, seg, n)
kernel_name = 'mk_rec_standalone_d1_rec_r8_ffe0c0'

def setup_inputs(seed: int=0):
    np.random.seed(seed)
    _w = jnp.asarray

    def _rec_inputs():
        import jax
        import jax.numpy as jnp
        _rk = jax.random.key(seed)
        r_xv = -9.80646e-05 + 1.00041 * jax.random.normal(jax.random.fold_in(_rk, 1), (2048, 32), jnp.float32)
        r_xi = jnp.stack([jax.random.randint(jax.random.fold_in(jax.random.fold_in(_rk, 2), 0), (2048,), 0, 1250, jnp.int32), jax.random.randint(jax.random.fold_in(jax.random.fold_in(_rk, 2), 1), (2048,), 0, 1250, jnp.int32), jax.random.randint(jax.random.fold_in(jax.random.fold_in(_rk, 2), 2), (2048,), 0, 1250, jnp.int32), jax.random.randint(jax.random.fold_in(jax.random.fold_in(_rk, 2), 3), (2048,), 3, 1250, jnp.int32), jax.random.randint(jax.random.fold_in(jax.random.fold_in(_rk, 2), 4), (2048,), 0, 1250, jnp.int32), jax.random.randint(jax.random.fold_in(jax.random.fold_in(_rk, 2), 5), (2048,), 0, 1250, jnp.int32), jax.random.randint(jax.random.fold_in(jax.random.fold_in(_rk, 2), 6), (2048,), 0, 1250, jnp.int32), jax.random.randint(jax.random.fold_in(jax.random.fold_in(_rk, 2), 7), (2048,), 0, 1250, jnp.int32), jax.random.randint(jax.random.fold_in(jax.random.fold_in(_rk, 2), 8), (2048,), 0, 1250, jnp.int32), jax.random.randint(jax.random.fold_in(jax.random.fold_in(_rk, 2), 9), (2048,), 0, 1250, jnp.int32), jax.random.randint(jax.random.fold_in(jax.random.fold_in(_rk, 2), 10), (2048,), 1, 1250, jnp.int32), jax.random.randint(jax.random.fold_in(jax.random.fold_in(_rk, 2), 11), (2048,), 1, 1250, jnp.int32), jax.random.randint(jax.random.fold_in(jax.random.fold_in(_rk, 2), 12), (2048,), 0, 9999, jnp.int32), jax.random.randint(jax.random.fold_in(jax.random.fold_in(_rk, 2), 13), (2048,), 0, 1250, jnp.int32), jax.random.randint(jax.random.fold_in(jax.random.fold_in(_rk, 2), 14), (2048,), 0, 1250, jnp.int32), jax.random.randint(jax.random.fold_in(jax.random.fold_in(_rk, 2), 15), (2048,), 2, 1250, jnp.int32), jax.random.randint(jax.random.fold_in(jax.random.fold_in(_rk, 2), 16), (2048,), 0, 1250, jnp.int32), jax.random.randint(jax.random.fold_in(jax.random.fold_in(_rk, 2), 17), (2048,), 0, 1250, jnp.int32), jax.random.randint(jax.random.fold_in(jax.random.fold_in(_rk, 2), 18), (2048,), 0, 1250, jnp.int32), jax.random.randint(jax.random.fold_in(jax.random.fold_in(_rk, 2), 19), (2048,), 0, 1250, jnp.int32), jax.random.randint(jax.random.fold_in(jax.random.fold_in(_rk, 2), 20), (2048,), 0, 1250, jnp.int32), jax.random.randint(jax.random.fold_in(jax.random.fold_in(_rk, 2), 21), (2048,), 0, 1250, jnp.int32), jax.random.randint(jax.random.fold_in(jax.random.fold_in(_rk, 2), 22), (2048,), 0, 1250, jnp.int32), jax.random.randint(jax.random.fold_in(jax.random.fold_in(_rk, 2), 23), (2048,), 0, 1250, jnp.int32), jax.random.randint(jax.random.fold_in(jax.random.fold_in(_rk, 2), 24), (2048,), 0, 1250, jnp.int32), jax.random.randint(jax.random.fold_in(jax.random.fold_in(_rk, 2), 25), (2048,), 1, 1250, jnp.int32), jax.random.randint(jax.random.fold_in(jax.random.fold_in(_rk, 2), 26), (2048,), 1, 1250, jnp.int32), jax.random.randint(jax.random.fold_in(jax.random.fold_in(_rk, 2), 27), (2048,), 2, 9999, jnp.int32), jax.random.randint(jax.random.fold_in(jax.random.fold_in(_rk, 2), 28), (2048,), 0, 1250, jnp.int32), jax.random.randint(jax.random.fold_in(jax.random.fold_in(_rk, 2), 29), (2048,), 0, 1250, jnp.int32), jax.random.randint(jax.random.fold_in(jax.random.fold_in(_rk, 2), 30), (2048,), 1, 1250, jnp.int32), jax.random.randint(jax.random.fold_in(jax.random.fold_in(_rk, 2), 31), (2048,), 0, 1250, jnp.int32)], axis=1)
        return (r_xv, r_xi)
    r_xv, r_xi = _rec_inputs()

    def _L0_rec_setup():
        import jax, jax.numpy as jnp
        import numpy as np
        F = 32
        V = 1250
        D = 496
        H = 1024
        OUT = 1
        B = 2048
        key = jax.random.key(seed)
        ks = jax.random.split(key, 8)
        xv = jax.random.normal(ks[0], (B, F), dtype=jnp.float32)
        xi = jax.random.randint(ks[1], (B, F), 0, V, dtype=jnp.int64)
        emb = jax.random.normal(ks[2], (F, V, D), dtype=jnp.float32) * 0.05
        W1 = jax.random.normal(ks[3], (F, H), dtype=jnp.float32) * (1.0 / np.sqrt(F))
        b1 = jax.random.normal(ks[4], (H,), dtype=jnp.float32) * 0.01
        W2 = jax.random.normal(ks[5], (H + D, OUT), dtype=jnp.float32) * (1.0 / np.sqrt(H + D))
        b2 = jax.random.normal(ks[6], (OUT,), dtype=jnp.float32) * 0.01
        return {'xv': xv, 'xi': xi, 'emb': emb, 'W1': W1, 'b1': b1, 'W2': W2, 'b2': b2}
    _L0_rec_all = _L0_rec_setup()
    _L0_rec_in = {k: v for k, v in _L0_rec_all.items() if k in ('emb', 'W1', 'b1', 'W2', 'b2')}
    del _L0_rec_all
    return {'r_xv': r_xv, 'r_xi': r_xi, 'L0_rec_emb': _L0_rec_in['emb'], 'L0_rec_W1': _L0_rec_in['W1'], 'L0_rec_b1': _L0_rec_in['b1'], 'L0_rec_W2': _L0_rec_in['W2'], 'L0_rec_b2': _L0_rec_in['b2']}

def reference(r_xv, r_xi, L0_rec_emb, L0_rec_W1, L0_rec_b1, L0_rec_W2, L0_rec_b2):
    import jax
    import jax.numpy as jnp

    def _L0_rec_ref(xv, xi, emb, W1, b1, W2, b2):
        import jax, jax.numpy as jnp
        import numpy as np
        F = 32
        V = 1250
        D = 496
        H = 1024
        OUT = 1
        B = 2048
        gathered = jax.vmap(lambda table, idx: table[idx], in_axes=(0, 1), out_axes=1)(emb, xi)
        e = gathered * xv[:, :, None]
        s = jnp.sum(e, axis=1)
        qi = 0.5 * (s * s - jnp.sum(e * e, axis=1))
        h = jax.nn.relu(xv @ W1 + b1)
        x = jnp.concatenate([qi, h], axis=1)
        return x @ W2 + b2
    y = _L0_rec_ref(r_xv, r_xi, L0_rec_emb, L0_rec_W1, L0_rec_b1, L0_rec_W2, L0_rec_b2)
    return y

_drawn_inputs = setup_inputs


def setup_inputs(seed=0):
    import zlib

    import numpy as np

    out = dict(_drawn_inputs(seed))
    spreads = {}
    factors = {'L0_rec_b1': 6.749}
    for name, (base, spread) in spreads.items():
        noise = np.random.default_rng([zlib.crc32(name.encode()), seed]).standard_normal(out[name].shape)
        drawn = base * np.exp(spread * noise) if base else spread * noise
        out[name] = jnp.asarray(drawn.astype(out[name].dtype))
    for name, factor in factors.items():
        out[name] = (out[name] * factor).astype(out[name].dtype)
    return out
```

```python
from contextlib import ExitStack

import concourse.bass as bass
from concourse import mybir

ALU = mybir.AluOpType
ACT = mybir.ActivationFunctionType
F32 = mybir.dt.float32
I32 = mybir.dt.int32

P = 128
GROUPS = 4
COLS = P // GROUPS


def fm_kernel(nc, index, value, value_t, emb, w1, b1, w2, b2, out):
    fields, batch = value_t.shape
    rows, dim = emb.shape
    vocab = rows // fields
    hidden = w1.shape[1]
    per = P // fields
    blocks = batch // P
    quads = P // (GROUPS * per)
    gathers = index.shape[1]
    in_block = quads * GROUPS
    halves = hidden // 512
    squares_ring = 4
    assert per * quads == COLS and gathers == blocks * in_block and dim <= 512

    with ExitStack() as ctx:
        def sb(name, shape, dt=F32):
            return ctx.enter_context(nc.sbuf_tensor(name, shape, dt))

        def psum(name, shape):
            return ctx.enter_context(nc.psum_tensor(name, shape, F32))

        def sem(name):
            return ctx.enter_context(nc.semaphore(name))

        index_raw = sb("index_raw", [P, gathers + in_block], I32)
        index_wrap = sb("index_wrap", [P, gathers + in_block])
        values = sb("values", [P, 2, gathers + in_block])
        first_row = sb("first_row", [P, 1])
        last_row = sb("last_row", [P, 1])
        own_row = sb("own_row", [P, per])
        index_now = sb("index_now", [P, quads, GROUPS], I32)
        weights = sb("weights", [P, 2, quads, GROUPS, COLS])
        gathered = sb("gathered", [P, quads, GROUPS, dim])
        squares = sb("squares", [P, squares_ring, GROUPS, dim])
        sum_squared = sb("sum_squared", [P, dim])
        interaction = sb("interaction", [P, dim])
        weighted = sb("weighted", [P, 1 + halves, 512])
        w2_all = sb("w2_all", [P, dim + hidden])
        b2_all = sb("b2_all", [P, 1])
        w1_b1 = sb("w1_b1", [fields + 1, hidden])
        value_rows = sb("value_rows", [fields + 1, batch])
        value_now = sb("value_now", [fields + 1, P])
        parts = sb("parts", [P, 1 + halves])
        y = sb("y", [P, COLS])
        y_t = sb("y_t", [P, COLS])

        sum_ps = psum("sum_ps", [P, 512])
        squares_ps = psum("squares_ps", [P, 512])
        hidden_ps = psum("hidden_ps", [P, halves, 512])

        index_loaded = sem("index_loaded")
        values_loaded = sem("values_loaded")
        w1_loaded = sem("w1_loaded")
        w2_loaded = sem("w2_loaded")
        rows_known = sem("rows_known")
        setup = sem("setup")
        index_ready = sem("index_ready")
        weights_ready = sem("weights_ready")
        fetched = [sem(f"fetched{s}") for s in range(quads)]
        quad_issued = sem("quad_issued")
        squared = sem("squared")
        summed = sem("summed")
        quad_done = sem("quad_done")
        sum_squared_ready = sem("sum_squared_ready")
        interaction_ready = sem("interaction_ready")
        value_now_ready = sem("value_now_ready")
        hidden_ready = sem("hidden_ready")
        hidden_used = sem("hidden_used")
        parts_ready = sem("parts_ready")
        y_ready = sem("y_ready")
        y_complete = sem("y_complete")
        stored = sem("stored")

        block = ctx.enter_context(nc.Block())

        @block.sync
        def _(sp):
            sp.dma_start(index_raw[:, 0:gathers], index).then_inc(index_loaded, 16)
            sp.dma_start(values[:, 0, 0:gathers], value).then_inc(values_loaded, 16)
            sp.dma_start(w1_b1[0:fields, :], w1).then_inc(w1_loaded, 16)
            sp.dma_start(w1_b1[fields:fields + 1, :], b1).then_inc(w1_loaded, 16)
            sp.dma_start(value_rows[0:fields, :], value_t).then_inc(w1_loaded, 16)
            sp.dma_start(w2_all[:], w2.rearrange("n o -> o n").to_broadcast([P, dim + hidden])
                         ).then_inc(w2_loaded, 16)
            sp.dma_start(b2_all[:], b2.to_broadcast([P, 1])).then_inc(w2_loaded, 16)
            sp.wait_ge(y_complete, 1)
            in_order = out.rearrange("(c r k) o -> r c (k o)", r=P // COLS, k=COLS)
            for r in range(P // COLS):
                sp.dma_start(in_order[r], y_t[r * COLS:r * COLS + blocks, :]).then_inc(stored, 16)
            sp.wait_ge(stored, 16 * (P // COLS))

        @block.gpsimd
        def _(pool):
            for b in range(per):
                nc.gpsimd.iota(first_row[b * fields:(b + 1) * fields, :], [[0, 1]], base=0,
                               channel_multiplier=vocab,
                               allow_small_or_imprecise_dtypes=True).then_inc(rows_known, 1)
            with pool.Fori(0, blocks) as i:
                for s in range(quads):
                    pool.wait_ge(index_ready, i * quads + (s + 1))
                    pool.sem_inc(quad_issued, 1)
                    for j in range(GROUPS):
                        nc.gpsimd.indirect_dma_start(
                            out=gathered[:, s, j, :], out_offset=None, in_=emb,
                            in_offset=bass.IndirectOffsetOnAxis(ap=index_now[:, s, j:j + 1], axis=0),
                        ).then_inc(fetched[s], 16)

        @block.scalar
        def _(act):
            with act.Fori(0, blocks) as i:
                for s in range(quads):
                    act.wait_ge(fetched[s], i * (16 * GROUPS) + 16 * GROUPS)
                    act.wait_ge(quad_done, i * quads + (s + 1))
                    nc.scalar.activation(squares[:, s % squares_ring], gathered[:, s],
                                         ACT.Square).then_inc(squared, 1)
                act.wait_ge(summed, i + 1)
                act.wait_ge(interaction_ready, i + 1)
                nc.scalar.activation(sum_squared[:], sum_ps[:, 0:dim],
                                     ACT.Square).then_inc(sum_squared_ready, 1)

        @block.tensor
        def _(pe):
            def sum_fields(s, which, source, bank):
                for j in range(GROUPS):
                    last = nc.tensor.matmul(bank[j * COLS:(j + 1) * COLS, 0:dim],
                                            weights[:, which, s, j, :], source[:, j, :],
                                            start=(s == 0), stop=(s == quads - 1),
                                            tile_position=(0, j * COLS))
                return last

            def sum_squares(i, s):
                pe.wait_ge(squared, i * quads + (s + 1))
                if s == 0:
                    pe.wait_ge(interaction_ready, i + 1)
                last = sum_fields(s, 1, squares[:, s % squares_ring], squares_ps)
                last.then_inc(quad_done, 1)

            pe.wait_ge(w1_loaded, 48)
            with pe.Fori(0, blocks) as i:
                for s in range(quads):
                    pe.wait_ge(weights_ready, i * quads + (s + 1))
                    pe.wait_ge(fetched[s], i * (16 * GROUPS) + 16 * GROUPS)
                    if s == 0:
                        pe.wait_ge(sum_squared_ready, i + 1)
                    last = sum_fields(s, 0, gathered[:, s], sum_ps)
                    if s == quads - 1:
                        last.then_inc(summed, 1)
                    if s > 0:
                        sum_squares(i, s - 1)
                    if s == quads // 2:
                        pe.wait_ge(value_now_ready, i + 1)
                        pe.wait_ge(hidden_used, i * halves + halves)
                        for h in range(halves):
                            last = nc.tensor.matmul(hidden_ps[:, h, :], value_now[:],
                                                    w1_b1[:, h * 512:(h + 1) * 512],
                                                    start=True, stop=True)
                        last.then_inc(hidden_ready, 1)
                sum_squares(i, quads - 1)

        @block.vector
        def _(dve):
            def refill(i, s):
                at = bass.ds(i * in_block + s * GROUPS, GROUPS)
                nc.vector.tensor_scalar(index_now[:, s, :], index_wrap[:, at], first_row[:],
                                        last_row[:], ALU.max, ALU.min).then_inc(index_ready, 1)
                nc.vector.tensor_tensor(
                    weights[:, :, s, :, s * per:(s + 1) * per],
                    values[:, :, at].unsqueeze(3).to_broadcast([P, 2, GROUPS, per]),
                    own_row[:].unsqueeze(1).unsqueeze(1).to_broadcast([P, 2, GROUPS, per]),
                    ALU.mult).then_inc(weights_ready, 1)

            nc.vector.memset(weights[:], 0.0)
            nc.vector.memset(own_row[:], 0.0).then_inc(setup, 1)
            nc.vector.memset(index_wrap[:, gathers:], 0.0)
            nc.vector.memset(values[:, :, gathers:], 0.0)
            nc.vector.memset(y[:], 0.0)
            nc.vector.memset(value_rows[fields:fields + 1, :], 1.0).then_inc(setup, 1)
            dve.wait_ge(setup, 2)
            for b in range(per):
                nc.vector.memset(own_row[b * fields:(b + 1) * fields, b:b + 1], 1.0).then_inc(setup, 1)
            dve.wait_ge(rows_known, per)
            nc.vector.tensor_scalar(last_row[:], first_row[:], float(vocab - 1), None,
                                    ALU.add).then_inc(setup, 1)
            dve.wait_ge(index_loaded, 16)
            nc.vector.tensor_scalar(index_wrap[:, 0:gathers], index_raw[:, 0:gathers], 0.0,
                                    float(vocab), ALU.is_lt, ALU.mult).then_inc(setup, 1)
            dve.wait_ge(setup, 4 + per)
            nc.vector.scalar_tensor_tensor(index_wrap[:, 0:gathers], index_wrap[:, 0:gathers],
                                           first_row[:], index_raw[:, 0:gathers], ALU.add,
                                           ALU.add).then_inc(setup, 1)
            dve.wait_ge(values_loaded, 16)
            nc.vector.tensor_tensor(values[:, 1, 0:gathers], values[:, 0, 0:gathers],
                                    values[:, 0, 0:gathers], ALU.mult).then_inc(setup, 1)
            dve.wait_ge(setup, 6 + per)
            for s in range(quads):
                refill(0, s)
            dve.wait_ge(w1_loaded, 48)
            dve.wait_ge(w2_loaded, 32)
            dve.sem_inc(quad_done, squares_ring)
            dve.sem_inc(sum_squared_ready, 1)
            dve.sem_inc(interaction_ready, 1)
            dve.sem_inc(hidden_used, halves)
            dve.sem_inc(y_ready, 1)

            with dve.Fori(0, blocks) as i:
                for s in range(quads):
                    dve.wait_ge(quad_done, i * quads + (squares_ring + s + 1))
                    refill(i + 1, s)
                    if s == 0:
                        nc.vector.tensor_copy(value_now[:], value_rows[:, bass.ds(i * P, P)]
                                              ).then_inc(value_now_ready, 1)
                    if s == quads // 2 + 1:
                        dve.wait_ge(hidden_ready, i + 1)
                        dve.wait_ge(hidden_used, i * halves + halves)
                        dve.wait_ge(y_ready, i + 1)
                        for h in range(halves):
                            nc.vector.scalar_tensor_tensor(
                                weighted[:, 1 + h, :], hidden_ps[:, h, :], 0.0,
                                w2_all[:, dim + h * 512:dim + (h + 1) * 512], ALU.max, ALU.mult,
                                accum_out=parts[:, 1 + h:2 + h]).then_inc(hidden_used, 1)
                dve.wait_ge(sum_squared_ready, i + 2)
                nc.vector.tensor_tensor(interaction[:], sum_squared[:], squares_ps[:, 0:dim],
                                        ALU.subtract).then_inc(interaction_ready, 1)
                dve.wait_ge(interaction_ready, i + 2)
                nc.vector.scalar_tensor_tensor(weighted[:, 0, 0:dim], interaction[:], 0.5,
                                               w2_all[:, 0:dim], ALU.mult, ALU.mult,
                                               accum_out=parts[:, 0:1]).then_inc(parts_ready, 1)
                dve.wait_ge(parts_ready, i + 1)
                dve.wait_ge(hidden_used, i * halves + 2 * halves)
                nc.vector.tensor_reduce(y[:, bass.ds(i, 1)], parts[:], mybir.AxisListType.X,
                                        ALU.add).then_inc(y_ready, 1)
            dve.wait_ge(y_ready, blocks + 1)
            nc.vector.tensor_scalar(y[:, 0:blocks], y[:, 0:blocks], b2_all[:], None,
                                    ALU.add).then_inc(y_ready, 1)
            dve.wait_ge(y_ready, blocks + 2)
            nc.vector.transpose(y_t[:], y[:]).then_inc(y_complete, 1)


def kernel(r_xv, r_xi, L0_rec_emb, L0_rec_W1, L0_rec_b1, L0_rec_W2, L0_rec_b2):
    import numpy as np
    import concourse.bacc as bacc
    from concourse.bass_utils import run_bass_kernel_spmd

    batch, fields = r_xv.shape
    per = P // fields
    quads = COLS // per

    def by_gather(a):
        a = np.asarray(a).reshape(batch // P, GROUPS, quads, per, fields)
        return np.ascontiguousarray(a.transpose(3, 4, 0, 2, 1).reshape(P, -1))

    emb = np.asarray(L0_rec_emb)
    arrays = {
        "index": by_gather(r_xi),
        "value": by_gather(r_xv),
        "value_t": np.ascontiguousarray(np.asarray(r_xv).T),
        "emb": emb.reshape(-1, emb.shape[2]),
        "w1": np.asarray(L0_rec_W1),
        "b1": np.asarray(L0_rec_b1).reshape(1, -1),
        "w2": np.asarray(L0_rec_W2),
        "b2": np.asarray(L0_rec_b2).reshape(1, 1),
    }
    nc = bacc.Bacc("TRN2", target_bir_lowering=False, num_devices=1)
    args = [nc.dram_tensor(n, a.shape, mybir.dt.from_np(a.dtype), kind="ExternalInput").ap()
            for n, a in arrays.items()]
    out = nc.dram_tensor("out", (batch, 1), F32, kind="ExternalOutput").ap()
    fm_kernel(nc, *args, out)
    return run_bass_kernel_spmd(nc, [arrays], core_ids=[0]).results[0]["out"]
```

```python
from contextlib import ExitStack

import concourse.bass as bass
from concourse import mybir

ALU = mybir.AluOpType
ACT = mybir.ActivationFunctionType
F32 = mybir.dt.float32
I32 = mybir.dt.int32

P = 128
GROUPS = 4
COLS = P // GROUPS


def fm_kernel(nc, index, value, value_t, emb, w1, b1, w2, b2, out):
    fields, batch = value_t.shape
    rows, dim = emb.shape
    vocab = rows // fields
    hidden = w1.shape[1]
    per = P // fields
    blocks = batch // P
    quads = P // (GROUPS * per)
    gathers = index.shape[1]
    in_block = quads * GROUPS
    halves = hidden // 512
    squares_ring = 4
    pair_arrived = 16 * GROUPS // 2
    assert per * quads == COLS and gathers == blocks * in_block and dim <= 512

    with ExitStack() as ctx:
        def sb(name, shape, dt=F32):
            return ctx.enter_context(nc.sbuf_tensor(name, shape, dt))

        def psum(name, shape):
            return ctx.enter_context(nc.psum_tensor(name, shape, F32))

        def sem(name):
            return ctx.enter_context(nc.semaphore(name))

        index_raw = sb("index_raw", [P, gathers], I32)
        index_wrap = sb("index_wrap", [P, gathers + in_block])
        values = sb("values", [P, 2, gathers + in_block])
        first_row = sb("first_row", [P, 1])
        last_row = sb("last_row", [P, 1])
        own_row = sb("own_row", [P, per])
        index_now = sb("index_now", [P, quads, GROUPS], I32)
        weights = sb("weights", [P, 2, quads, GROUPS, COLS])
        gathered = sb("gathered", [P, quads, GROUPS, dim])
        squares = sb("squares", [P, squares_ring, GROUPS, dim])
        weighted = sb("weighted", [P, 2 + halves, 512])
        w2_all = sb("w2_all", [P, dim + hidden])
        w1_b1 = sb("w1_b1", [fields + 1, hidden])
        value_rows = sb("value_rows", [fields + 1, batch])
        value_now = sb("value_now", [fields + 1, P])
        parts = sb("parts", [P, 3 + halves])
        y = sb("y", [P, blocks])

        sum_ps = psum("sum_ps", [P, 512])
        squares_ps = psum("squares_ps", [P, 512])
        sum_squared = psum("sum_squared", [P, 512])
        hidden_ps = psum("hidden_ps", [P, halves, 512])

        first_loaded = sem("first_loaded")
        index_loaded = sem("index_loaded")
        values_loaded = sem("values_loaded")
        w1_loaded = sem("w1_loaded")
        w2_loaded = sem("w2_loaded")
        rows_known = sem("rows_known")
        setup = sem("setup")
        index_ready = sem("index_ready")
        weights_ready = sem("weights_ready")
        fetched = [[sem(f"fetched{s}_{half}") for half in range(2)] for s in range(quads)]
        quad_issued = sem("quad_issued")
        squared = sem("squared")
        summed = sem("summed")
        quad_done = sem("quad_done")
        sum_squared_ready = sem("sum_squared_ready")
        sum_squared_used = sem("sum_squared_used")
        squares_used = sem("squares_used")
        value_now_ready = sem("value_now_ready")
        hidden_ready = sem("hidden_ready")
        hidden_used = sem("hidden_used")
        y_ready = sem("y_ready")
        stored = sem("stored")

        block = ctx.enter_context(nc.Block())

        @block.sync
        def _(sp):
            sp.dma_start(index_raw[:, 0:in_block], index[:, 0:in_block]).then_inc(first_loaded, 16)
            sp.dma_start(values[:, 0, 0:gathers], value).then_inc(values_loaded, 16)
            sp.dma_start(index_raw[:, in_block:gathers], index[:, in_block:]
                         ).then_inc(index_loaded, 16)
            sp.dma_start(w2_all[:], w2.rearrange("n o -> o n").to_broadcast([P, dim + hidden])
                         ).then_inc(w2_loaded, 16)
            sp.dma_start(parts[:, 2 + halves:], b2.to_broadcast([P, 1])).then_inc(w2_loaded, 16)
            by_block = out.rearrange("(c p) o -> p (c o)", p=P)
            with sp.Fori(0, blocks) as i:
                sp.wait_ge(y_ready, i + 2)
                sp.dma_start(by_block[:, bass.ds(i, 1)], y[:, bass.ds(i, 1)]).then_inc(stored, 16)
            sp.wait_ge(stored, 16 * blocks)

        @block.gpsimd
        def _(pool):
            for b in range(per):
                nc.gpsimd.iota(first_row[b * fields:(b + 1) * fields, :], [[0, 1]], base=0,
                               channel_multiplier=vocab,
                               allow_small_or_imprecise_dtypes=True).then_inc(rows_known, 1)
            with pool.Fori(0, blocks) as i:
                for s in range(quads):
                    pool.wait_ge(index_ready, i * quads + (s + 1))
                    pool.sem_inc(quad_issued, 1)
                    for j in range(GROUPS):
                        nc.gpsimd.indirect_dma_start(
                            out=gathered[:, s, j, :], out_offset=None, in_=emb,
                            in_offset=bass.IndirectOffsetOnAxis(ap=index_now[:, s, j:j + 1], axis=0),
                        ).then_inc(fetched[s][j // 2], 16)

        @block.scalar
        def _(act):
            act.dma_start(w1_b1[0:fields, :], w1).then_inc(w1_loaded, 16)
            act.dma_start(w1_b1[fields:fields + 1, :], b1).then_inc(w1_loaded, 16)
            act.dma_start(value_rows[0:fields, :], value_t).then_inc(w1_loaded, 16)
            with act.Fori(0, blocks) as i:
                for s in range(quads):
                    act.wait_ge(quad_done, i * quads + (s + 1))
                    for half in range(2):
                        pair = slice(2 * half, 2 * half + 2)
                        act.wait_ge(fetched[s][half], i * pair_arrived + pair_arrived)
                        nc.scalar.activation(squares[:, s % squares_ring, pair],
                                             gathered[:, s, pair], ACT.Square).then_inc(squared, 1)
                act.wait_ge(summed, i + 1)
                act.wait_ge(sum_squared_used, i + 1)
                nc.scalar.activation(sum_squared[:, 0:dim], sum_ps[:, 0:dim],
                                     ACT.Square).then_inc(sum_squared_ready, 1)

        @block.tensor
        def _(pe):
            def sum_fields(s, which, source, bank):
                for j in range(GROUPS):
                    last = nc.tensor.matmul(bank[j * COLS:(j + 1) * COLS, 0:dim],
                                            weights[:, which, s, j, :], source[:, j, :],
                                            start=(s == 0), stop=(s == quads - 1),
                                            tile_position=(0, j * COLS))
                return last

            def sum_squares(i, s):
                pe.wait_ge(squared, i * (2 * quads) + 2 * (s + 1))
                if s == 0:
                    pe.wait_ge(squares_used, i + 1)
                last = sum_fields(s, 1, squares[:, s % squares_ring], squares_ps)
                last.then_inc(quad_done, 1)

            pe.wait_ge(w1_loaded, 48)
            with pe.Fori(0, blocks) as i:
                for s in range(quads):
                    pe.wait_ge(weights_ready, i * quads + (s + 1))
                    for half in range(2):
                        pe.wait_ge(fetched[s][half], i * pair_arrived + pair_arrived)
                    if s == 0:
                        pe.wait_ge(sum_squared_ready, i + 1)
                    last = sum_fields(s, 0, gathered[:, s], sum_ps)
                    if s == quads - 1:
                        last.then_inc(summed, 1)
                    sum_squares(i, s)
                    if s == quads // 2:
                        pe.wait_ge(value_now_ready, i + 1)
                        pe.wait_ge(hidden_used, i * halves + halves)
                        for h in range(halves):
                            last = nc.tensor.matmul(hidden_ps[:, h, :], value_now[:],
                                                    w1_b1[:, h * 512:(h + 1) * 512],
                                                    start=True, stop=True)
                        last.then_inc(hidden_ready, 1)

        @block.vector
        def _(dve):
            def at(i, s):
                return bass.ds(i * in_block + s * GROUPS, GROUPS)

            def refill_index(i, s):
                nc.vector.tensor_scalar(index_now[:, s, :], index_wrap[:, at(i, s)], first_row[:],
                                        last_row[:], ALU.max, ALU.min).then_inc(index_ready, 1)

            def refill_weights(i, s):
                nc.vector.tensor_tensor(
                    weights[:, :, s, :, s * per:(s + 1) * per],
                    values[:, :, at(i, s)].unsqueeze(3).to_broadcast([P, 2, GROUPS, per]),
                    own_row[:].unsqueeze(1).unsqueeze(1).to_broadcast([P, 2, GROUPS, per]),
                    ALU.mult).then_inc(weights_ready, 1)

            done = [0]

            def step(instruction):
                done[0] += 1
                instruction.then_inc(setup, 1)
                dve.wait_ge(setup, done[0])

            def wrap(columns):
                step(nc.vector.tensor_scalar(index_wrap[:, columns], index_raw[:, columns], 0.0,
                                             float(vocab), ALU.is_lt, ALU.mult))
                step(nc.vector.scalar_tensor_tensor(
                    index_wrap[:, columns], index_wrap[:, columns], first_row[:],
                    index_raw[:, columns], ALU.add, ALU.add))

            dve.wait_ge(rows_known, per)
            step(nc.vector.tensor_scalar(last_row[:], first_row[:], float(vocab - 1), None, ALU.add))
            dve.wait_ge(first_loaded, 16)
            wrap(slice(0, in_block))
            for s in range(quads):
                refill_index(0, s)
            nc.vector.memset(weights[:], 0.0)
            nc.vector.memset(index_wrap[:, gathers:], 0.0)
            nc.vector.memset(values[:, :, gathers:], 0.0)
            step(nc.vector.memset(own_row[:], 0.0))
            dve.sem_inc(quad_done, squares_ring)
            dve.sem_inc(sum_squared_ready, 1)
            dve.sem_inc(sum_squared_used, 1)
            dve.sem_inc(squares_used, 1)
            dve.sem_inc(hidden_used, halves)
            dve.sem_inc(y_ready, 1)
            for b in range(per):
                nc.vector.memset(own_row[b * fields:(b + 1) * fields, b:b + 1], 1.0)
            dve.wait_ge(values_loaded, 16)
            step(nc.vector.tensor_tensor(values[:, 1, 0:gathers], values[:, 0, 0:gathers],
                                         values[:, 0, 0:gathers], ALU.mult))
            for s in range(quads):
                refill_weights(0, s)
            dve.wait_ge(index_loaded, 16)
            wrap(slice(in_block, gathers))
            step(nc.vector.memset(value_rows[fields:fields + 1, :], 1.0))
            dve.wait_ge(w1_loaded, 48)
            dve.wait_ge(w2_loaded, 32)

            with dve.Fori(0, blocks) as i:
                for s in range(quads):
                    dve.wait_ge(quad_done, i * quads + (squares_ring + s + 1))
                    if s == quads - 1:
                        nc.vector.scalar_tensor_tensor(
                            weighted[:, 1, 0:dim], squares_ps[:, 0:dim], -0.5, w2_all[:, 0:dim],
                            ALU.mult, ALU.mult, accum_out=parts[:, 1:2]).then_inc(squares_used, 1)
                        dve.wait_ge(hidden_used, i * halves + 2 * halves)
                        dve.wait_ge(sum_squared_used, i + 2)
                        dve.wait_ge(squares_used, i + 2)
                        nc.vector.tensor_reduce(y[:, bass.ds(i, 1)], parts[:],
                                                mybir.AxisListType.X, ALU.add).then_inc(y_ready, 1)
                    refill_index(i + 1, s)
                    refill_weights(i + 1, s)
                    if s == 0:
                        nc.vector.tensor_copy(value_now[:], value_rows[:, bass.ds(i * P, P)]
                                              ).then_inc(value_now_ready, 1)
                    if s == quads // 2 + 1:
                        dve.wait_ge(hidden_ready, i + 1)
                        dve.wait_ge(hidden_used, i * halves + halves)
                        dve.wait_ge(y_ready, i + 1)
                        for h in range(halves):
                            nc.vector.scalar_tensor_tensor(
                                weighted[:, 2 + h, :], hidden_ps[:, h, :], 0.0,
                                w2_all[:, dim + h * 512:dim + (h + 1) * 512], ALU.max, ALU.mult,
                                accum_out=parts[:, 2 + h:3 + h]).then_inc(hidden_used, 1)
                    if s == quads - 2:
                        dve.wait_ge(sum_squared_ready, i + 2)
                        nc.vector.scalar_tensor_tensor(
                            weighted[:, 0, 0:dim], sum_squared[:, 0:dim], 0.5, w2_all[:, 0:dim],
                            ALU.mult, ALU.mult, accum_out=parts[:, 0:1]
                        ).then_inc(sum_squared_used, 1)


def kernel(r_xv, r_xi, L0_rec_emb, L0_rec_W1, L0_rec_b1, L0_rec_W2, L0_rec_b2):
    import numpy as np
    import concourse.bacc as bacc
    from concourse.bass_utils import run_bass_kernel_spmd

    batch, fields = r_xv.shape
    per = P // fields
    quads = COLS // per

    def by_gather(a):
        a = np.asarray(a).reshape(batch // P, GROUPS, quads, per, fields)
        return np.ascontiguousarray(a.transpose(3, 4, 0, 2, 1).reshape(P, -1))

    emb = np.asarray(L0_rec_emb)
    arrays = {
        "index": by_gather(r_xi),
        "value": by_gather(r_xv),
        "value_t": np.ascontiguousarray(np.asarray(r_xv).T),
        "emb": emb.reshape(-1, emb.shape[2]),
        "w1": np.asarray(L0_rec_W1),
        "b1": np.asarray(L0_rec_b1).reshape(1, -1),
        "w2": np.asarray(L0_rec_W2),
        "b2": np.asarray(L0_rec_b2).reshape(1, 1),
    }
    nc = bacc.Bacc("TRN2", target_bir_lowering=False, num_devices=1)
    args = [nc.dram_tensor(n, a.shape, mybir.dt.from_np(a.dtype), kind="ExternalInput").ap()
            for n, a in arrays.items()]
    out = nc.dram_tensor("out", (batch, 1), F32, kind="ExternalOutput").ap()
    fm_kernel(nc, *args, out)
    return run_bass_kernel_spmd(nc, [arrays], core_ids=[0]).results[0]["out"]
```
